# Optimizing a Trainium2 kernel written in Bass

```python
import numpy as np
import jax
import jax.numpy as jnp

def _softmax(x, axis=-1):
    return jax.nn.softmax(x, axis=axis)

def _gelu(x):
    return jax.nn.gelu(x, approximate=True)

def _silu(x):
    return jax.nn.silu(x)

def _sigmoid(x):
    return jax.nn.sigmoid(x)

def _layernorm(x, axis=-1, eps=1e-05):
    m = jnp.mean(x, axis=axis, keepdims=True)
    v = jnp.var(x, axis=axis, keepdims=True)
    return (x - m) / jnp.sqrt(v + eps)

def _scatter_add(tgt, idx, src, axis=0):
    return tgt.at[idx].add(src)

def _segment_sum(src, seg, n):
    return jax.ops.segment_sum(src, seg, n)
kernel_name = 'mk_dlrm_tower_d1_rec_r8_0af57e'

def setup_inputs(seed: int=0):
    np.random.seed(seed)
    _w = jnp.asarray

    def _rec_inputs():
        import jax
        import jax.numpy as jnp
        _tk = jax.random.key(seed)
        ids = jnp.stack([jax.random.randint(jax.random.fold_in(_tk, 200 + f), (2048,), 0, v, jnp.int32) for f, v in enumerate([1000, 12500, 1250, 125000, 1000, 12500, 1250, 1250, 1000, 12500, 12500, 12500, 1000, 1250, 1000, 1000, 12500, 12500, 1250, 12500, 1250, 1250, 1250, 1000, 1250, 1250, 1000])], axis=1)
        tbl_0 = 0.05 * jax.random.normal(jax.random.fold_in(_tk, 500 + 0), (1000, 128), jnp.float32)
        tbl_1 = 0.05 * jax.random.normal(jax.random.fold_in(_tk, 500 + 1), (12500, 128), jnp.float32)
        tbl_2 = 0.05 * jax.random.normal(jax.random.fold_in(_tk, 500 + 2), (1250, 128), jnp.float32)
        tbl_3 = 0.05 * jax.random.normal(jax.random.fold_in(_tk, 500 + 3), (125000, 128), jnp.float32)
        tbl_4 = 0.05 * jax.random.normal(jax.random.fold_in(_tk, 500 + 4), (1000, 128), jnp.float32)
        tbl_5 = 0.05 * jax.random.normal(jax.random.fold_in(_tk, 500 + 5), (12500, 128), jnp.float32)
        tbl_6 = 0.05 * jax.random.normal(jax.random.fold_in(_tk, 500 + 6), (1250, 128), jnp.float32)
        tbl_7 = 0.05 * jax.random.normal(jax.random.fold_in(_tk, 500 + 7), (1250, 128), jnp.float32)
        tbl_8 = 0.05 * jax.random.normal(jax.random.fold_in(_tk, 500 + 8), (1000, 128), jnp.float32)
        tbl_9 = 0.05 * jax.random.normal(jax.random.fold_in(_tk, 500 + 9), (12500, 128), jnp.float32)
        tbl_10 = 0.05 * jax.random.normal(jax.random.fold_in(_tk, 500 + 10), (12500, 128), jnp.float32)
        tbl_11 = 0.05 * jax.random.normal(jax.random.fold_in(_tk, 500 + 11), (12500, 128), jnp.float32)
        tbl_12 = 0.05 * jax.random.normal(jax.random.fold_in(_tk, 500 + 12), (1000, 128), jnp.float32)
        tbl_13 = 0.05 * jax.random.normal(jax.random.fold_in(_tk, 500 + 13), (1250, 128), jnp.float32)
        tbl_14 = 0.05 * jax.random.normal(jax.random.fold_in(_tk, 500 + 14), (1000, 128), jnp.float32)
        tbl_15 = 0.05 * jax.random.normal(jax.random.fold_in(_tk, 500 + 15), (1000, 128), jnp.float32)
        tbl_16 = 0.05 * jax.random.normal(jax.random.fold_in(_tk, 500 + 16), (12500, 128), jnp.float32)
        tbl_17 = 0.05 * jax.random.normal(jax.random.fold_in(_tk, 500 + 17), (12500, 128), jnp.float32)
        tbl_18 = 0.05 * jax.random.normal(jax.random.fold_in(_tk, 500 + 18), (1250, 128), jnp.float32)
        tbl_19 = 0.05 * jax.random.normal(jax.random.fold_in(_tk, 500 + 19), (12500, 128), jnp.float32)
        tbl_20 = 0.05 * jax.random.normal(jax.random.fold_in(_tk, 500 + 20), (1250, 128), jnp.float32)
        tbl_21 = 0.05 * jax.random.normal(jax.random.fold_in(_tk, 500 + 21), (1250, 128), jnp.float32)
        tbl_22 = 0.05 * jax.random.normal(jax.random.fold_in(_tk, 500 + 22), (1250, 128), jnp.float32)
        tbl_23 = 0.05 * jax.random.normal(jax.random.fold_in(_tk, 500 + 23), (1000, 128), jnp.float32)
        tbl_24 = 0.05 * jax.random.normal(jax.random.fold_in(_tk, 500 + 24), (1250, 128), jnp.float32)
        tbl_25 = 0.05 * jax.random.normal(jax.random.fold_in(_tk, 500 + 25), (1250, 128), jnp.float32)
        tbl_26 = 0.05 * jax.random.normal(jax.random.fold_in(_tk, 500 + 26), (1000, 128), jnp.float32)
        _rk = jax.random.fold_in(_tk, 7)
        r_bottom_mlp_out = 4.13588e-05 + 0.999923 * jax.random.normal(jax.random.fold_in(_rk, 101), (2048, 128), jnp.float32)
        W_top1 = 0.0405887 * jax.random.normal(jax.random.fold_in(_tk, 801), (607, 512), jnp.float32)
        W_top2 = 0.0441942 * jax.random.normal(jax.random.fold_in(_tk, 802), (512, 256), jnp.float32)
        W_top3 = 0.0625 * jax.random.normal(jax.random.fold_in(_tk, 803), (256, 1), jnp.float32)
        b_top1 = jnp.zeros((512,), jnp.float32)
        b_top2 = jnp.zeros((256,), jnp.float32)
        return (r_bottom_mlp_out, ids, tbl_0, tbl_1, tbl_2, tbl_3, tbl_4, tbl_5, tbl_6, tbl_7, tbl_8, tbl_9, tbl_10, tbl_11, tbl_12, tbl_13, tbl_14, tbl_15, tbl_16, tbl_17, tbl_18, tbl_19, tbl_20, tbl_21, tbl_22, tbl_23, tbl_24, tbl_25, tbl_26, W_top1, b_top1, W_top2, b_top2, W_top3)
    r_bottom_mlp_out, ids, tbl_0, tbl_1, tbl_2, tbl_3, tbl_4, tbl_5, tbl_6, tbl_7, tbl_8, tbl_9, tbl_10, tbl_11, tbl_12, tbl_13, tbl_14, tbl_15, tbl_16, tbl_17, tbl_18, tbl_19, tbl_20, tbl_21, tbl_22, tbl_23, tbl_24, tbl_25, tbl_26, W_top1, b_top1, W_top2, b_top2, W_top3 = _rec_inputs()

    def _L0_rec_setup():
        import jax, jax.numpy as jnp
        import numpy as np
        NUM_FEATURES = 27

        def _tril_indices(F):
            idx = []
            for i in range(F):
                for j in range(i):
                    idx.append(i * F + j)
            return np.asarray(idx, dtype=np.int32)
        TRIL_IDX = _tril_indices(NUM_FEATURES)
        key = jax.random.key(seed)
        k1, k2 = jax.random.split(key)
        B, F, D = (8192, NUM_FEATURES, 128)
        features = jax.random.normal(k1, (B, F, D), dtype=jnp.float32)
        bottom_mlp_out = jax.random.normal(k2, (B, D), dtype=jnp.float32)
        return {'features': features, 'bottom_mlp_out': bottom_mlp_out}
    _L0_rec_all = _L0_rec_setup()
    _L0_rec_in = {k: v for k, v in _L0_rec_all.items() if k in ()}
    del _L0_rec_all
    return {'r_bottom_mlp_out': r_bottom_mlp_out, 'ids': ids, 'tbl_0': tbl_0, 'tbl_1': tbl_1, 'tbl_2': tbl_2, 'tbl_3': tbl_3, 'tbl_4': tbl_4, 'tbl_5': tbl_5, 'tbl_6': tbl_6, 'tbl_7': tbl_7, 'tbl_8': tbl_8, 'tbl_9': tbl_9, 'tbl_10': tbl_10, 'tbl_11': tbl_11, 'tbl_12': tbl_12, 'tbl_13': tbl_13, 'tbl_14': tbl_14, 'tbl_15': tbl_15, 'tbl_16': tbl_16, 'tbl_17': tbl_17, 'tbl_18': tbl_18, 'tbl_19': tbl_19, 'tbl_20': tbl_20, 'tbl_21': tbl_21, 'tbl_22': tbl_22, 'tbl_23': tbl_23, 'tbl_24': tbl_24, 'tbl_25': tbl_25, 'tbl_26': tbl_26, 'W_top1': W_top1, 'b_top1': b_top1, 'W_top2': W_top2, 'b_top2': b_top2, 'W_top3': W_top3}

def reference(r_bottom_mlp_out, ids, tbl_0, tbl_1, tbl_2, tbl_3, tbl_4, tbl_5, tbl_6, tbl_7, tbl_8, tbl_9, tbl_10, tbl_11, tbl_12, tbl_13, tbl_14, tbl_15, tbl_16, tbl_17, tbl_18, tbl_19, tbl_20, tbl_21, tbl_22, tbl_23, tbl_24, tbl_25, tbl_26, W_top1, b_top1, W_top2, b_top2, W_top3):
    import jax
    import jax.numpy as jnp

    def _L0_rec_ref(features, bottom_mlp_out):
        import jax, jax.numpy as jnp
        import numpy as np
        NUM_FEATURES = 27

        def _tril_indices(F):
            idx = []
            for i in range(F):
                for j in range(i):
                    idx.append(i * F + j)
            return np.asarray(idx, dtype=np.int32)
        TRIL_IDX = _tril_indices(NUM_FEATURES)
        B = features.shape[0]
        F = features.shape[1]
        interactions = jnp.einsum('bfd,bgd->bfg', features, features)
        interactions = interactions.reshape(B, F * F)
        x = interactions[:, TRIL_IDX]
        return jnp.concatenate([bottom_mlp_out, x], axis=1)
    e = jnp.stack([tbl_0[ids[:, 0]], tbl_1[ids[:, 1]], tbl_2[ids[:, 2]], tbl_3[ids[:, 3]], tbl_4[ids[:, 4]], tbl_5[ids[:, 5]], tbl_6[ids[:, 6]], tbl_7[ids[:, 7]], tbl_8[ids[:, 8]], tbl_9[ids[:, 9]], tbl_10[ids[:, 10]], tbl_11[ids[:, 11]], tbl_12[ids[:, 12]], tbl_13[ids[:, 13]], tbl_14[ids[:, 14]], tbl_15[ids[:, 15]], tbl_16[ids[:, 16]], tbl_17[ids[:, 17]], tbl_18[ids[:, 18]], tbl_19[ids[:, 19]], tbl_20[ids[:, 20]], tbl_21[ids[:, 21]], tbl_22[ids[:, 22]], tbl_23[ids[:, 23]], tbl_24[ids[:, 24]], tbl_25[ids[:, 25]], tbl_26[ids[:, 26]]], axis=1)
    z = _L0_rec_ref(e, r_bottom_mlp_out)
    z = z.reshape(z.shape[0], -1)
    h = jnp.concatenate([z, r_bottom_mlp_out], axis=1)
    h = jnp.maximum(h @ W_top1 + b_top1, 0.0)
    h = jnp.maximum(h @ W_top2 + b_top2, 0.0)
    y = h @ W_top3
    return y

_drawn_inputs = setup_inputs


def setup_inputs(seed=0):
    import zlib

    import numpy as np

    out = dict(_drawn_inputs(seed))
    spreads = {'b_top1': (0.0, 0.1), 'b_top2': (0.0, 0.1)}
    factors = {'tbl_0': 4.814,
     'tbl_1': 5.115,
     'tbl_2': 4.435,
     'tbl_3': 4.078,
     'tbl_4': 4.742,
     'tbl_5': 4.479,
     'tbl_6': 4.946,
     'tbl_7': 4.196,
     'tbl_8': 4.596,
     'tbl_9': 4.935,
     'tbl_10': 4.397,
     'tbl_11': 4.657,
     'tbl_12': 4.541,
     'tbl_13': 4.353,
     'tbl_14': 4.649,
     'tbl_15': 4.95,
     'tbl_16': 4.77,
     'tbl_17': 4.954,
     'tbl_18': 4.184,
     'tbl_19': 4.291,
     'tbl_20': 4.373,
     'tbl_21': 4.833,
     'tbl_22': 4.613,
     'tbl_23': 4.921,
     'tbl_24': 4.393,
     'tbl_25': 4.892,
     'tbl_26': 4.622}
    for name, (base, spread) in spreads.items():
        noise = np.random.default_rng([zlib.crc32(name.encode()), seed]).standard_normal(out[name].shape)
        drawn = base * np.exp(spread * noise) if base else spread * noise
        out[name] = jnp.asarray(drawn.astype(out[name].dtype))
    for name, factor in factors.items():
        out[name] = (out[name] * factor).astype(out[name].dtype)
    return out
```

```python
import concourse.bass as bass
from concourse import mybir
from contextlib import ExitStack

B = 2048
F = 27
D = 128
VOCAB = [1000, 12500, 1250, 125000, 1000, 12500, 1250, 1250, 1000, 12500, 12500, 12500, 1000, 1250,
         1000, 1000, 12500, 12500, 1250, 12500, 1250, 1250, 1250, 1000, 1250, 1250, 1000]
N1, N2 = 512, 256
PAIRS = F * (F - 1) // 2

ONE_HOT = 7
SMALL = min(VOCAB)
ONE_HOT_TABLES = [f for f in range(F) if VOCAB[f] == SMALL][-ONE_HOT:]
GATHERED_TABLES = [f for f in range(F) if f not in ONE_HOT_TABLES]
GATHERED = len(GATHERED_TABLES)
ORDER = GATHERED_TABLES + ONE_HOT_TABLES

TILE = 256
TILES = B // TILE
HALF = 128
CHUNKS = 8
ROWS = SMALL // CHUNKS
PARTS = 3
MASKS = 4
STAGES = 3
PAD = 32
PACK = 4
SET = 32
SETS = TILE // SET
GROUP = 4
X_CHUNKS = -(-PAIRS // 128)
X_ROWS = [min(128, PAIRS - 128 * c) for c in range(X_CHUNKS)]


def groups_of_tile():
    lookups = [("mask", 0, k, min(2, ONE_HOT - k)) for k in range(0, ONE_HOT, 2)]
    halves = [[("gather", h, f, min(GROUP, GATHERED - f)) for f in range(0, GATHERED, GROUP)] for h in range(2)]
    return lookups, halves[0], halves[1]


LOOKUPS, HALF0, HALF1 = groups_of_tile()
FILLS = len(LOOKUPS) + len(HALF0) + len(HALF1)
assert FILLS % 2 == 0
PER_BANK = FILLS // 2


def pair_moves():
    moves = []
    for i in range(1, F):
        row, j = i * (i - 1) // 2, 0
        while j < i:
            n = min(i - j, 128 - row % 128)
            moves.append((i, j, n, row // 128, row % 128))
            row, j = row + n, j + n
    return moves


MOVES = pair_moves()
MOVES_OF_CHUNK = [sum(m[3] == c for m in MOVES) for c in range(X_CHUNKS)]


def build(nc, tables, idx_d, hot_ids_d, bottom_d, w1_d, wa_d, wb_d, b1_d, w2_d, b2_d, w3_d, ident_d, rowid_d, out_d):
    fp32, bf16, fp16, i32 = mybir.dt.float32, mybir.dt.bfloat16, mybir.dt.float16, mybir.dt.int32
    ALU = mybir.AluOpType
    ACT = mybir.ActivationFunctionType

    ctx = ExitStack()
    with ctx:
        def sb(name, shape, dt):
            return ctx.enter_context(nc.sbuf_tensor(name, shape, dt))

        def sem(name):
            return ctx.enter_context(nc.semaphore(name))

        idx = sb("idx", [128, 4, GATHERED], i32)
        rows = sb("rows", [128, 2, GATHERED * D], fp32)
        eT = sb("eT", [128, TILE, PAD], fp32)
        pairs = sb("pairs", [128, (F - 1) * TILE], fp32)
        stage = pairs[:, 0:STAGES * CHUNKS * D].rearrange("p (s n) -> p s n", s=STAGES)
        x = sb("x", [128, X_CHUNKS + 1, TILE], fp32)
        parts = sb("parts", [128, ONE_HOT, PARTS, CHUNKS * D], bf16)
        mask = sb("mask", [128, MASKS, CHUNKS, TILE], bf16)
        hot_i = sb("hot_i", [128, ONE_HOT, TILE], i32)
        hot_f = sb("hot_f", [128, ONE_HOT, TILE], fp16)
        rowid = sb("rowid", [128, CHUNKS], fp32)
        ident = sb("ident", [128, 128], fp32)
        w1 = sb("w1", [128, X_CHUNKS + 1, N1], fp32)
        wb = sb("wb", [128, N1], fp32)
        w2 = sb("w2", [128, N1 // 128, N2], fp32)
        w3 = sb("w3", [128, N2 // 128], fp32)
        b1 = sb("b1", [128, N1 // 128], fp32)
        b2 = sb("b2", [128, N2 // 128], fp32)
        h1 = sb("h1", [128, N1 // 128, TILE], fp32)
        h2 = sb("h2", [128, N2 // 128, TILE], fp32)
        y = sb("y", [1, TILE], fp32)

        col_bank = [ctx.enter_context(nc.psum_tensor(f"col_bank{b}", [128, 512], fp32)) for b in range(2)]
        gram_bank = [ctx.enter_context(nc.psum_tensor(f"gram_bank{b}", [128, SET // PACK, 128], fp32)) for b in range(2)]
        mlp_bank = [ctx.enter_context(nc.psum_tensor(f"mlp_bank{b}", [128, 2, TILE], fp32)) for b in range(2)]

        idx_loaded = [sem(f"idx_loaded{s}") for s in range(4)]
        gathered = [sem(f"gathered{h}") for h in range(2)]
        half_transposed = [sem(f"half_transposed{h}") for h in range(2)]
        consts_loaded = sem("consts_loaded")
        weights_loaded = sem("weights_loaded")
        w1_summed = sem("w1_summed")
        pads_cleared = sem("pads_cleared")
        table_loaded = [sem(f"table_loaded{s}") for s in range(STAGES)]
        high_made = sem("high_made")
        rest_made = sem("rest_made")
        middle_made = sem("middle_made")
        low_made = sem("low_made")
        hot_ids_loaded = sem("hot_ids_loaded")
        hot_ids_cast = sem("hot_ids_cast")
        masks_made = sem("masks_made")
        looked_up = sem("looked_up")
        col_full = [sem(f"col_full{b}") for b in range(2)]
        col_copied = [sem(f"col_copied{b}") for b in range(2)]
        gram_full = [sem(f"gram_full{b}") for b in range(2)]
        gram_copied = [sem(f"gram_copied{b}") for b in range(2)]
        x_loaded = [sem(f"x_loaded{c}") for c in range(X_CHUNKS + 1)]
        l1_full = sem("l1_full")
        h1_made = sem("h1_made")
        l2_full = sem("l2_full")
        h2_made = sem("h2_made")
        l3_full = sem("l3_full")
        y_made = sem("y_made")
        y_stored = sem("y_stored")

        def columns_of(group):
            kind, h, f, n = group
            if kind == "mask":
                return eT[:, :, GATHERED + f:GATHERED + f + n].rearrange("p s f -> p f s")
            return eT[:, h * HALF:(h + 1) * HALF, f:f + n].rearrange("p s f -> p f s")

        def filled(b, group):
            width = TILE if group[0] == "mask" else HALF
            return col_bank[b][:, 0:group[3] * width].rearrange("p (f s) -> p f s", f=group[3])

        def pairs_of(s, j):
            return pairs[0:F - 1, :].rearrange("p (g s) -> p s g", s=TILE)[:, s * SET + j:(s + 1) * SET:PACK, :]

        def gram_of(b, j):
            return gram_bank[b][32 * j:32 * j + F - 1, :, j * (F - 1):(j + 1) * (F - 1)]

        g0, g1 = len(LOOKUPS), len(LOOKUPS) + len(HALF0)
        counted = [[g for g, _ in enumerate(HALF0, g0) if g != g1 - 1 and g % 2 == b]
                   + [g for g, _ in enumerate(HALF1, g1) if g != FILLS - 1 and g % 2 == b] for b in range(2)]

        def fill_signal(t, g, group):
            kind, h, f, n = group
            if kind == "mask":
                return looked_up, t * ONE_HOT + f + n
            if g in (g1 - 1, FILLS - 1):
                return half_transposed[h], t + 2
            return col_full[g % 2], t * len(counted[g % 2]) + counted[g % 2].index(g) + 1

        block = ctx.enter_context(nc.Block())

        @block.gpsimd
        def _(pool):
            for h in range(2):
                pool.sem_inc(half_transposed[h], 1)
            with pool.Fori(0, TILES // 2) as u:
                for par in range(2):
                    for h in range(2):
                        pool.wait_ge(idx_loaded[2 * par + h], u * 16 + 16)
                        pool.wait_ge(half_transposed[h], u * 2 + (par + 1))
                        pool.nop(nofuse=True)
                        for n, f in enumerate(GATHERED_TABLES):
                            pool.indirect_dma_start(
                                out=rows[:, h, n * D:(n + 1) * D], out_offset=None, in_=tables[f],
                                in_offset=bass.IndirectOffsetOnAxis(ap=idx[:, 2 * par + h, n:n + 1], axis=0),
                            ).then_inc(gathered[h], 16)

        @block.sync
        def _(sp):
            def load_idx(t, slot):
                sp.dma_start(idx[:, slot, :], idx_d[bass.ds(t * 2 + slot % 2, 1)].rearrange("a p f -> (a p) f"))\
                    .then_inc(idx_loaded[slot], 16)

            def load_hot_ids(t):
                src = hot_ids_d[bass.ds(t, 1)].rearrange("a k s -> a (k s)").broadcast_to([128, ONE_HOT * TILE])
                sp.dma_start(hot_i[:, :, :].rearrange("p k s -> p (k s)"), src).then_inc(hot_ids_loaded, 16)

            def load_x(t, later):
                if later:
                    sp.wait_ge(l1_full, t * 2)
                sp.dma_start(x[:, X_CHUNKS, :], bottom_d[:, bass.ds(t * TILE, TILE)]).then_inc(x_loaded[X_CHUNKS], 16)
                for b in range(2):
                    sp.wait_ge(gram_copied[b], t * (SETS // 2) + SETS // 2)
                for i, j, n, c, row in MOVES:
                    sp.dma_start(x[row:row + n, c, :], pairs[j:j + n, (i - 1) * TILE:i * TILE])\
                        .then_inc(x_loaded[c], 16)

            def store_y(t):
                sp.wait_ge(y_made, t + 1)
                sp.dma_start(out_d[bass.ds(t, 1), :], y[0:1, :]).then_inc(y_stored, 16)

            for slot in range(4):
                load_idx(slot // 2, slot)
            sp.dma_start(rowid[:, :], rowid_d).then_inc(consts_loaded, 16)
            sp.dma_start(ident[:, :], ident_d).then_inc(consts_loaded, 16)
            load_hot_ids(0)
            for k, f in enumerate(ONE_HOT_TABLES):
                if k >= STAGES:
                    sp.wait_ge(low_made, k - STAGES + 1)
                sp.dma_start(stage[0:ROWS, k % STAGES, :], tables[f].rearrange("(p c) d -> p (c d)", c=CHUNKS))\
                    .then_inc(table_loaded[k % STAGES], 16)
            sp.wait_ge(hot_ids_cast, 1)
            load_hot_ids(1)
            load_x(0, False)
            load_idx(2, 0)
            load_idx(2, 1)

            def tile(t, next_ids, next_slots):
                if next_ids:
                    sp.wait_ge(hot_ids_cast, t + 1)
                    load_hot_ids(t + 1)
                store_y(t - 1)
                load_x(t, True)
                for slot in next_slots:
                    load_idx(t + 2, slot)

            with sp.Fori(0, (TILES - 4) // 2) as u:
                tile(u * 2 + 1, True, (2, 3))
                tile(u * 2 + 2, True, (0, 1))
            tile(TILES - 3, True, (2, 3))
            tile(TILES - 2, True, ())
            tile(TILES - 1, False, ())
            store_y(TILES - 1)
            sp.wait_ge(y_stored, 16 * TILES)

        @block.scalar
        def _(act):
            act.dma_start(w1[:, X_CHUNKS, :], wa_d).then_inc(weights_loaded, 16)
            act.dma_start(wb[:, :], wb_d).then_inc(weights_loaded, 16)
            for c in range(X_CHUNKS):
                act.dma_start(w1[0:X_ROWS[c], c, :], w1_d[128 * c:128 * c + X_ROWS[c], :]).then_inc(weights_loaded, 16)
            act.dma_start(w2[:, :, :], w2_d.rearrange("(c p) n -> p c n", p=128)).then_inc(weights_loaded, 16)
            act.dma_start(w3[:, :], w3_d).then_inc(weights_loaded, 16)
            act.dma_start(b1[:, :], b1_d).then_inc(weights_loaded, 16)
            act.dma_start(b2[:, :], b2_d).then_inc(weights_loaded, 16)

            def cast_ids(t):
                act.wait_ge(hot_ids_loaded, t * 16 + 16)
                act.wait_ge(masks_made, t * ONE_HOT)
                nc.scalar.activation(hot_f[:, :, :], hot_i[:, :, :], ACT.Copy).then_inc(hot_ids_cast, 1)

            act.wait_ge(hot_ids_loaded, 16)
            nc.scalar.activation(hot_f[:, :, :], hot_i[:, :, :], ACT.Copy).then_inc(hot_ids_cast, 1)
            for k in range(ONE_HOT + 1):
                if k < ONE_HOT:
                    act.wait_ge(table_loaded[k % STAGES], 16 * (k // STAGES) + 16)
                    nc.scalar.activation(parts[0:ROWS, k, 0, :], stage[0:ROWS, k % STAGES, :], ACT.Copy).then_inc(high_made, 1)
                if k == 0:
                    continue
                k = k - 1
                act.wait_ge(rest_made, k + 1)
                nc.scalar.activation(parts[0:ROWS, k, 1, :], stage[0:ROWS, k % STAGES, :], ACT.Copy).then_inc(middle_made, 1)
            act.wait_ge(weights_loaded, 16 * 9)

            def copy_columns(t, first, groups):
                for g, group in enumerate(groups, first):
                    if g % 2 == 1:
                        act.wait_ge(*fill_signal(t, g, group))
                        nc.scalar.activation(columns_of(group), filled(1, group), ACT.Copy).then_inc(col_copied[1], 1)

            def copy_pairs(t, later):
                if later:
                    for c in range(X_CHUNKS):
                        act.wait_ge(x_loaded[c], t * (16 * MOVES_OF_CHUNK[c]))
                else:
                    act.wait_ge(low_made, ONE_HOT)
                for s in range(1, SETS, 2):
                    act.wait_ge(gram_full[1], t * (SETS // 2) + s // 2 + 1)
                    for j in range(PACK):
                        last = nc.scalar.activation(pairs_of(s, j), gram_of(1, j), ACT.Copy)
                    last.then_inc(gram_copied[1], 1)

            def relu1(t):
                for b in range(2):
                    act.wait_ge(l1_full, t * 2 + b + 1)
                    for m in range(2):
                        last = nc.scalar.activation(h1[:, 2 * b + m, :], mlp_bank[b][:, m, :], ACT.Relu,
                                                    bias=b1[:, 2 * b + m:2 * b + m + 1])
                    last.then_inc(h1_made, 1)

            def relu2(t):
                act.wait_ge(l2_full, t + 1)
                for m in range(2):
                    last = nc.scalar.activation(h2[:, m, :], mlp_bank[0][:, m, :], ACT.Relu, bias=b2[:, m:m + 1])
                last.then_inc(h2_made, 1)

            def copy_y(t, later):
                act.wait_ge(l3_full, t + 1)
                if later:
                    act.wait_ge(y_stored, t * 16)
                nc.scalar.activation(y[0:1, :], mlp_bank[1][0:1, 0, :], ACT.Copy).then_inc(y_made, 1)

            copy_columns(0, 0, LOOKUPS)
            copy_columns(0, g0, HALF0)
            cast_ids(1)
            copy_columns(0, g1, HALF1)
            copy_pairs(0, False)

            def tile(t, last, y_later):
                copy_columns(t, 0, LOOKUPS)
                relu1(t - 1)
                copy_columns(t, g0, HALF0)
                relu2(t - 1)
                if not last:
                    cast_ids(t + 1)
                copy_columns(t, g1, HALF1)
                copy_y(t - 1, y_later)
                copy_pairs(t, True)

            tile(1, False, False)
            with act.Fori(2, TILES - 1) as t:
                tile(t, False, True)
            tile(TILES - 1, True, True)
            relu1(TILES - 1)
            relu2(TILES - 1)
            copy_y(TILES - 1, True)

        @block.vector
        def _(dve):
            nc.vector.memset(eT[:, :, F:PAD], 0.0).then_inc(pads_cleared, 1)

            def make_mask(t, k, chunks, later=True):
                if chunks[0] == 0:
                    dve.wait_ge(hot_ids_cast, t + 1)
                    if k >= MASKS:
                        dve.wait_ge(looked_up, t * ONE_HOT + (k - MASKS + 1))
                    elif later:
                        before = max(range(k, ONE_HOT, MASKS))
                        dve.wait_ge(looked_up, t * ONE_HOT - (ONE_HOT - before - 1))
                for c in chunks:
                    last = nc.vector.tensor_scalar(mask[0:ROWS, k % MASKS, c, :], hot_f[0:ROWS, k, :],
                                                   rowid[0:ROWS, c:c + 1], None, ALU.is_equal)
                if chunks[-1] == CHUNKS - 1:
                    last.then_inc(masks_made, 1)

            dve.wait_ge(consts_loaded, 32)
            for k in range(ONE_HOT):
                table = stage[0:ROWS, k % STAGES, :]
                dve.wait_ge(high_made, k + 1)
                nc.vector.tensor_tensor(table, table, parts[0:ROWS, k, 0, :], ALU.subtract).then_inc(rest_made, 1)
                if k < MASKS:
                    make_mask(0, k, range(CHUNKS), False)
                dve.wait_ge(middle_made, k + 1)
                nc.vector.tensor_tensor(parts[0:ROWS, k, 2, :], table, parts[0:ROWS, k, 1, :], ALU.subtract)\
                    .then_inc(low_made, 1)
            dve.wait_ge(weights_loaded, 16 * 9)
            nc.vector.tensor_tensor(w1[:, X_CHUNKS, :], w1[:, X_CHUNKS, :], wb[:, :], ALU.add).then_inc(w1_summed, 1)

            def copy_columns(t, first, groups, masks_from=None):
                k = masks_from
                for g, group in enumerate(groups, first):
                    if g % 2 == 0:
                        while k is not None and k < min(ONE_HOT, 2 * g + MASKS):
                            make_mask(t, k, range(CHUNKS))
                            k += 1
                        dve.wait_ge(*fill_signal(t, g, group))
                        nc.vector.tensor_copy(columns_of(group), filled(0, group)).then_inc(col_copied[0], 1)

            def copy_pairs(t, later, with_masks):
                if later:
                    for c in range(X_CHUNKS):
                        dve.wait_ge(x_loaded[c], t * (16 * MOVES_OF_CHUNK[c]))
                for s in range(0, SETS, 2):
                    dve.wait_ge(gram_full[0], t * (SETS // 2) + s // 2 + 1)
                    for j in range(PACK):
                        last = nc.vector.tensor_copy(pairs_of(s, j), gram_of(0, j))
                    last.then_inc(gram_copied[0], 1)
                    if with_masks:
                        make_mask(t + 1, s // 4, range(s // 2 % 2 * 4, s // 2 % 2 * 4 + 4))

            def tile(t, later, last):
                copy_columns(t, 0, LOOKUPS, 2 if later else MASKS)
                copy_columns(t, g0, HALF0)
                copy_columns(t, g1, HALF1)
                copy_pairs(t, later, not last)

            tile(0, False, False)
            with dve.Fori(1, TILES - 1) as t:
                tile(t, True, False)
            tile(TILES - 1, True, True)

        @block.tensor
        def _(pe):
            def look_up(t, later):
                for g, (_, _, f, n) in enumerate(LOOKUPS):
                    b = g % 2
                    if later or g >= 2:
                        pe.wait_ge(col_copied[b], t * PER_BANK + g // 2)
                    for i in range(n):
                        k = f + i
                        if not later:
                            pe.wait_ge(low_made, k + 1)
                        pe.wait_ge(masks_made, t * ONE_HOT + k + 1)
                        for c in range(CHUNKS):
                            for part in range(PARTS):
                                last = nc.tensor.matmul(
                                    col_bank[b][:, i * TILE:(i + 1) * TILE], parts[0:ROWS, k, part, c * D:(c + 1) * D],
                                    mask[0:ROWS, k % MASKS, c, :], start=(c == 0 and part == 0),
                                    stop=(c == CHUNKS - 1 and part == PARTS - 1))
                        last.then_inc(looked_up, 1)

            def transpose_rows(t, h, first, groups):
                pe.wait_ge(gathered[h], t * (16 * GATHERED) + 16 * GATHERED)
                for g, (_, _, f, n) in enumerate(groups, first):
                    b = g % 2
                    pe.wait_ge(col_copied[b], t * PER_BANK + g // 2)
                    for i in range(n):
                        last = nc.tensor.transpose(col_bank[b][:, i * HALF:(i + 1) * HALF],
                                                   rows[:, h, (f + i) * D:(f + i + 1) * D], ident[:, :])
                    last.then_inc(half_transposed[h] if f + n == GATHERED else col_full[b], 1)

            def multiply_pairs(t, later):
                for b in range(2):
                    pe.wait_ge(col_copied[b], t * PER_BANK + PER_BANK)
                for s in range(SETS):
                    if later or s >= 2:
                        pe.wait_ge(gram_copied[s % 2], t * (SETS // 2) + s // 2)
                    for q in range(SET // PACK):
                        a = s * SET + q * PACK
                        last = nc.tensor.matmul(gram_bank[s % 2][:, q, 0:PACK * (F - 1)],
                                                eT[:, a:a + PACK, :].rearrange("p s f -> p (s f)"),
                                                eT[:, a:a + PACK, 1:F], start=True, stop=True)
                    last.then_inc(gram_full[s % 2], 1)

            def layer1(t, later):
                for b in range(2):
                    if b == 1 and later:
                        pe.wait_ge(y_made, t)
                    for m in range(2):
                        for c in range(X_CHUNKS + 1):
                            if b == 0 and m == 0:
                                moves = MOVES_OF_CHUNK[c] if c < X_CHUNKS else 1
                                pe.wait_ge(x_loaded[c], t * (16 * moves) + 16 * moves)
                            n = X_ROWS[c] if c < X_CHUNKS else D
                            a = (2 * b + m) * 128
                            last = nc.tensor.matmul(mlp_bank[b][:, m, :], w1[0:n, c, a:a + 128], x[0:n, c, :],
                                                    start=(c == 0), stop=(c == X_CHUNKS))
                    last.then_inc(l1_full, 1)

            def layer2(t):
                pe.wait_ge(h1_made, t * 2 + 2)
                for m in range(2):
                    for c in range(N1 // 128):
                        last = nc.tensor.matmul(mlp_bank[0][:, m, :], w2[:, c, m * 128:(m + 1) * 128], h1[:, c, :],
                                                start=(c == 0), stop=(c == N1 // 128 - 1))
                last.then_inc(l2_full, 1)

            def layer3(t):
                pe.wait_ge(h2_made, t + 1)
                for c in range(N2 // 128):
                    last = nc.tensor.matmul(mlp_bank[1][0:1, 0, :], w3[:, c:c + 1], h2[:, c, :],
                                            start=(c == 0), stop=(c == N2 // 128 - 1))
                last.then_inc(l3_full, 1)

            pe.wait_ge(consts_loaded, 32)
            look_up(0, False)
            transpose_rows(0, 0, g0, HALF0)
            transpose_rows(0, 1, g1, HALF1)
            pe.wait_ge(pads_cleared, 1)
            multiply_pairs(0, False)
            pe.wait_ge(weights_loaded, 16 * 9)
            pe.wait_ge(w1_summed, 1)

            def tile(t, l1_later):
                look_up(t, True)
                layer1(t - 1, l1_later)
                transpose_rows(t, 0, g0, HALF0)
                layer2(t - 1)
                transpose_rows(t, 1, g1, HALF1)
                layer3(t - 1)
                multiply_pairs(t, True)

            tile(1, False)
            with pe.Fori(2, TILES) as t:
                tile(t, True)
            layer1(TILES - 1, True)
            layer2(TILES - 1)
            layer3(TILES - 1)


def kernel(**inputs):
    import numpy as np
    import concourse.bacc as bacc
    from concourse.bass_utils import run_bass_kernel_spmd

    nc = bacc.Bacc("TRN2", target_bir_lowering=False, num_devices=1)
    arrays = {}

    def put(name, a):
        a = np.ascontiguousarray(a)
        arrays[name] = a
        return nc.dram_tensor(name, a.shape, mybir.dt.from_np(a.dtype), kind="ExternalInput").ap()

    ids = np.asarray(inputs["ids"])
    w_top1 = np.asarray(inputs["W_top1"])
    pair_rows = [D + max(ORDER[i], ORDER[j]) * (max(ORDER[i], ORDER[j]) - 1) // 2 + min(ORDER[i], ORDER[j])
                 for i in range(F) for j in range(i)]
    tables = [put(f"in_tbl_{f}", inputs[f"tbl_{f}"]) for f in range(F)]
    args = [
        put("in_gather_ids", ids[:, GATHERED_TABLES].reshape(B // HALF, HALF, GATHERED)),
        put("in_hot_ids", ids[:, ONE_HOT_TABLES].reshape(TILES, TILE, ONE_HOT).transpose(0, 2, 1)),
        put("in_bottom", np.asarray(inputs["r_bottom_mlp_out"]).T),
        put("in_w1_pairs", w_top1[pair_rows]),
        put("in_w1_bottom_a", w_top1[0:D]),
        put("in_w1_bottom_b", w_top1[D + PAIRS:]),
        put("in_b1", np.asarray(inputs["b_top1"]).reshape(N1 // 128, 128).T),
        put("in_w2", inputs["W_top2"]),
        put("in_b2", np.asarray(inputs["b_top2"]).reshape(N2 // 128, 128).T),
        put("in_w3", np.asarray(inputs["W_top3"]).reshape(N2 // 128, 128).T),
        put("in_identity", np.eye(128, dtype=np.float32)),
        put("in_row_of_chunk", np.arange(128 * CHUNKS, dtype=np.float32).reshape(128, CHUNKS)),
    ]
    out = nc.dram_tensor("out_y", (TILES, TILE), mybir.dt.float32, kind="ExternalOutput").ap()
    build(nc, tables, *args, out)
    r = run_bass_kernel_spmd(nc, [arrays], core_ids=[0])
    return r.results[0]["out_y"].reshape(B, 1)
```

```python
import concourse.bass as bass
from concourse import mybir
from contextlib import ExitStack

B = 2048
F = 27
D = 128
VOCAB = [1000, 12500, 1250, 125000, 1000, 12500, 1250, 1250, 1000, 12500, 12500, 12500, 1000, 1250,
         1000, 1000, 12500, 12500, 1250, 12500, 1250, 1250, 1250, 1000, 1250, 1250, 1000]
N1, N2 = 512, 256
PAIRS = F * (F - 1) // 2

ONE_HOT = 7
SMALL = min(VOCAB)
ONE_HOT_TABLES = [f for f in range(F) if VOCAB[f] == SMALL][-ONE_HOT:]
GATHERED_TABLES = [f for f in range(F) if f not in ONE_HOT_TABLES]
GATHERED = len(GATHERED_TABLES)
ORDER = GATHERED_TABLES + ONE_HOT_TABLES

TILE = 256
TILES = B // TILE
HALF = 128
CHUNKS = 8
ROWS = SMALL // CHUNKS
PARTS = 2
MASKS = 4
STAGES = 3
PAD = 32
GRAM_ROWS = 3 * PAD + F - 1
PACK = 4
SET = 32
SETS = HALF // SET
GROUP = 4
X_CHUNKS = 3
WEIGHT_LOADS = 6 + X_CHUNKS


def spread(count, most):
    n = -(-count // most)
    sizes = [count // n + (i < count % n) for i in range(n)]
    return [(sum(sizes[:i]), size) for i, size in enumerate(sizes)]


def fills_of_tile():
    gathers = [[("gather", h, f, n) for f, n in spread(GATHERED, GROUP)] for h in range(2)]
    lookups = [("mask", 0, f, n) for f, n in spread(ONE_HOT, 2)]
    if len(lookups) % 2:
        _, _, f, n = lookups.pop()
        lookups += [("mask", 0, f, 1), ("mask", 0, f + 1, 1)]
    return lookups, gathers[0], gathers[1]


LOOKUPS, HALF0, HALF1 = fills_of_tile()
G0, G1, FILLS = len(LOOKUPS), len(LOOKUPS) + len(HALF0), len(LOOKUPS) + 2 * len(HALF0)
assert FILLS % 2 == 0
PER_BANK = FILLS // 2

BLOCKS = [(F - X_CHUNKS - 3 * r, F - 1 - 3 * r) for r in range(-(-(F - 1) // X_CHUNKS))]
BLOCK_ROW = [sum(n for _, n in BLOCKS[:r]) for r in range(len(BLOCKS))]
X_ROWS = [sum(n for i, n in BLOCKS if i + c > 0) for c in range(X_CHUNKS)]
assert max(X_ROWS) <= 128


def build(nc, tables, idx_d, hot_ids_d, bottom_d, w1_d, wa_d, wb_d, b1_d, w2_d, b2_d, w3_d, ident_d, rowid_d, out_d):
    fp32, bf16, fp16, i32 = mybir.dt.float32, mybir.dt.bfloat16, mybir.dt.float16, mybir.dt.int32
    ALU = mybir.AluOpType
    ACT = mybir.ActivationFunctionType

    ctx = ExitStack()
    with ctx:
        def sb(name, shape, dt):
            return ctx.enter_context(nc.sbuf_tensor(name, shape, dt))

        def ps(name, shape):
            return ctx.enter_context(nc.psum_tensor(name, shape, fp32))

        def sem(name):
            return ctx.enter_context(nc.semaphore(name))

        idx = sb("idx", [128, 4, GATHERED], i32)
        rows = sb("rows", [128, 2, GATHERED * D], fp32)
        eT = sb("eT", [128, TILE, PAD], fp32)
        pairs = sb("pairs", [128, (F - 1) * TILE], fp32)
        stage = pairs[:, 0:STAGES * CHUNKS * D].rearrange("p (s n) -> p s n", s=STAGES)
        x = sb("x", [128, X_CHUNKS + 1, TILE], fp32)
        f32r = mybir.dt.float32r
        parts = sb("parts", [128, ONE_HOT, PARTS, CHUNKS * D], f32r)
        mask = sb("mask", [128, MASKS, CHUNKS, TILE], f32r)
        hot_i = sb("hot_i", [128, ONE_HOT, TILE], i32)
        hot_f = sb("hot_f", [128, ONE_HOT, TILE], fp16)
        rowid = sb("rowid", [128, CHUNKS], fp32)
        ident = sb("ident", [128, 128], fp32)
        w1 = sb("w1", [128, X_CHUNKS + 1, N1], fp32)
        wb = sb("wb", [128, N1], fp32)
        w2 = sb("w2", [128, N1 // 128, N2], fp32)
        w3 = sb("w3", [128, N2 // 128], fp32)
        b1 = sb("b1", [128, N1 // 128], fp32)
        b2 = sb("b2", [128, N2 // 128], fp32)
        h1 = sb("h1", [128, N1 // 128, TILE], fp32)
        h2 = sb("h2", [128, N2 // 128, TILE], fp32)
        y = sb("y", [1, TILE], fp32)

        col_bank = [ps(f"col_bank{b}", [128, 512]) for b in range(2)]
        gram_bank = [ps(f"gram_bank{b}", [128, SET // PACK, 128]) for b in range(2)]
        mlp_bank = [ps(f"mlp_bank{b}", [128, 2, TILE]) for b in range(2)]

        idx_loaded = [sem(f"idx_loaded{s}") for s in range(4)]
        gathered = [sem(f"gathered{h}") for h in range(2)]
        half_transposed = [sem(f"half_transposed{h}") for h in range(2)]
        rowid_loaded = sem("rowid_loaded")
        ident_loaded = sem("ident_loaded")
        weights_loaded = sem("weights_loaded")
        w1_summed = sem("w1_summed")
        pads_cleared = sem("pads_cleared")
        table_loaded = [sem(f"table_loaded{s}") for s in range(STAGES)]
        high_made = sem("high_made")
        rest_made = sem("rest_made")
        middle_made = sem("middle_made")
        low_made = sem("low_made")
        hot_ids_loaded = sem("hot_ids_loaded")
        hot_ids_cast = sem("hot_ids_cast")
        masks_made = sem("masks_made")
        looked_up = sem("looked_up")
        col_full = [sem(f"col_full{b}") for b in range(2)]
        col_copied = [sem(f"col_copied{b}") for b in range(2)]
        gram_full = [sem(f"gram_full{b}") for b in range(2)]
        gram_copied = [sem(f"gram_copied{b}") for b in range(2)]
        x_loaded = [sem(f"x_loaded{h}") for h in range(2)]
        bottom_loaded = sem("bottom_loaded")
        l1_full = sem("l1_full")
        h1_made = sem("h1_made")
        l2_full = sem("l2_full")
        h2_made = sem("h2_made")
        l3_full = sem("l3_full")
        y_made = sem("y_made")
        y_stored = sem("y_stored")

        def columns_of(group):
            kind, h, f, n = group
            if kind == "mask":
                return eT[:, :, GATHERED + f:GATHERED + f + n].rearrange("p s f -> p f s")
            return eT[:, h * HALF:(h + 1) * HALF, f:f + n].rearrange("p s f -> p f s")

        def filled(b, group):
            width = TILE if group[0] == "mask" else HALF
            return col_bank[b][:, 0:group[3] * width].rearrange("p (f s) -> p f s", f=group[3])

        def pairs_of(h, s, j):
            first = h * HALF + s * SET
            return pairs[0:F - 1, :].rearrange("p (g s) -> p s g", s=TILE)[:, first + j:first + SET:PACK, :]

        def gram_of(b, j):
            return gram_bank[b][PAD * j:PAD * j + F - 1, :, j * (F - 1):(j + 1) * (F - 1)]

        counted = [[g for g in range(G0, FILLS) if g not in (G1 - 1, FILLS - 1) and g % 2 == b] for b in range(2)]

        def fill_signal(t, g, group):
            kind, h, f, n = group
            if kind == "mask":
                return looked_up, t * ONE_HOT + (f + n)
            if g in (G1 - 1, FILLS - 1):
                return half_transposed[h], t + 2
            return col_full[g % 2], t * len(counted[g % 2]) + (counted[g % 2].index(g) + 1)

        block = ctx.enter_context(nc.Block())

        @block.gpsimd
        def _(pool):
            for h in range(2):
                pool.sem_inc(half_transposed[h], 1)
            with pool.Fori(0, TILES // 2) as u:
                for par in range(2):
                    for h in range(2):
                        pool.wait_ge(idx_loaded[2 * par + h], u * 16 + 16)
                        pool.wait_ge(half_transposed[h], u * 2 + (par + 1))
                        pool.nop(nofuse=True)
                        for n, f in enumerate(GATHERED_TABLES):
                            pool.indirect_dma_start(
                                out=rows[:, h, n * D:(n + 1) * D], out_offset=None, in_=tables[f],
                                in_offset=bass.IndirectOffsetOnAxis(ap=idx[:, 2 * par + h, n:n + 1], axis=0),
                            ).then_inc(gathered[h], 16)

        @block.sync
        def _(sp):
            def load_idx(t, slot):
                sp.dma_start(idx[:, slot, :], idx_d[bass.ds(t * 2 + slot % 2, 1)].rearrange("a p f -> (a p) f"))\
                    .then_inc(idx_loaded[slot], 16)

            def load_hot_ids(t):
                src = hot_ids_d[bass.ds(t, 1)].rearrange("a k s -> a (k s)").broadcast_to([128, ONE_HOT * TILE])
                sp.dma_start(hot_i[:, :, :].rearrange("p k s -> p (k s)"), src).then_inc(hot_ids_loaded, 16)

            def load_bottom(t):
                sp.dma_start(x[:, X_CHUNKS, :], bottom_d[:, bass.ds(t * TILE, TILE)]).then_inc(bottom_loaded, 16)

            def load_x(t, h):
                for b in range(2):
                    sp.wait_ge(gram_copied[b], t * SETS + (h + 1) * SETS // 2)
                for (i, n), row in zip(BLOCKS, BLOCK_ROW):
                    c = max(0, 1 - i)
                    src = pairs[0:n, (i + c - 1) * TILE:(i + X_CHUNKS - 1) * TILE].rearrange("p (c s) -> p c s", s=TILE)
                    sp.dma_start(x[row:row + n, c:X_CHUNKS, h * HALF:(h + 1) * HALF],
                                 src[:, :, h * HALF:(h + 1) * HALF]).then_inc(x_loaded[h], 16)

            def store_y(n, at, size):
                sp.wait_ge(y_made, n + 1)
                sp.dma_start(out_d[:, bass.ds(at, size)], y[0:1, 0:size]).then_inc(y_stored, 16)

            load_idx(0, 0)
            sp.dma_start(stage[0:ROWS, 0, :], tables[ONE_HOT_TABLES[0]].rearrange("(p c) d -> p (c d)", c=CHUNKS))\
                .then_inc(table_loaded[0], 16)
            load_hot_ids(0)
            sp.dma_start(rowid[:, :], rowid_d).then_inc(rowid_loaded, 16)
            for k, f in enumerate(ONE_HOT_TABLES):
                if k == STAGES:
                    sp.dma_start(ident[:, :], ident_d).then_inc(ident_loaded, 16)
                    for slot in range(1, 4):
                        load_idx(slot // 2, slot)
                if k >= STAGES:
                    sp.wait_ge(low_made, k - STAGES + 1)
                if k > 0:
                    sp.dma_start(stage[0:ROWS, k % STAGES, :], tables[f].rearrange("(p c) d -> p (c d)", c=CHUNKS))\
                        .then_inc(table_loaded[k % STAGES], 16)
            sp.dma_start(w1[:, X_CHUNKS, :], wa_d).then_inc(weights_loaded, 16)
            sp.dma_start(wb[:, :], wb_d).then_inc(weights_loaded, 16)
            for c in range(X_CHUNKS):
                sp.dma_start(w1[0:X_ROWS[c], c, :], w1_d[0:X_ROWS[c], c * N1:(c + 1) * N1]).then_inc(weights_loaded, 16)
            sp.dma_start(w2[:, :, :], w2_d.rearrange("(c p) n -> p c n", p=128)).then_inc(weights_loaded, 16)
            sp.dma_start(w3[:, :], w3_d).then_inc(weights_loaded, 16)
            sp.dma_start(b1[:, :], b1_d).then_inc(weights_loaded, 16)
            sp.dma_start(b2[:, :], b2_d).then_inc(weights_loaded, 16)
            sp.wait_ge(hot_ids_cast, 1)
            load_hot_ids(1)
            load_bottom(0)
            load_x(0, 0)
            load_x(0, 1)
            load_idx(2, 0)
            load_idx(2, 1)

            def tile(t, next_ids, next_slots, last=False):
                if next_ids:
                    sp.wait_ge(hot_ids_cast, t + 1)
                    load_hot_ids(t + 1)
                sp.wait_ge(l1_full, t * 2)
                load_bottom(t)
                load_x(t, 0)
                if last:
                    store_y(t - 1, (t - 1) * TILE, TILE)
                    store_y(t, t * TILE, HALF)
                    load_x(t, 1)
                else:
                    load_x(t, 1)
                    store_y(t - 1, (t - 1) * TILE, TILE)
                for slot in next_slots:
                    load_idx(t + 2, slot)

            with sp.Fori(0, (TILES - 4) // 2) as u:
                tile(u * 2 + 1, True, (2, 3))
                tile(u * 2 + 2, True, (0, 1))
            tile(TILES - 3, True, (2, 3))
            tile(TILES - 2, True, ())
            tile(TILES - 1, False, (), True)
            store_y(TILES, B - HALF, HALF)
            sp.wait_ge(y_stored, 16 * (TILES + 1))

        @block.scalar
        def _(act):
            def cast_ids(t):
                act.wait_ge(hot_ids_loaded, t * 16 + 16)
                act.wait_ge(masks_made, t * ONE_HOT)
                nc.scalar.activation(hot_f[:, :, :], hot_i[:, :, :], ACT.Copy).then_inc(hot_ids_cast, 1)

            def make_high(k):
                act.wait_ge(table_loaded[k % STAGES], 16 * (k // STAGES) + 16)
                nc.scalar.activation(parts[0:ROWS, k, 0, :], stage[0:ROWS, k % STAGES, :], ACT.Copy).then_inc(high_made, 1)

            def make_middle(k):
                act.wait_ge(rest_made, k + 1)
                nc.scalar.activation(parts[0:ROWS, k, 1, :], stage[0:ROWS, k % STAGES, :], ACT.Copy).then_inc(middle_made, 1)

            def copy_columns(t, first, groups):
                for g, group in enumerate(groups, first):
                    if g % 2 == 1:
                        act.wait_ge(*fill_signal(t, g, group))
                        nc.scalar.activation(columns_of(group), filled(1, group), ACT.Copy).then_inc(col_copied[1], 1)

            def copy_pairs(t, h, later):
                if later:
                    act.wait_ge(x_loaded[h], t * (16 * len(BLOCKS)))
                else:
                    act.wait_ge(low_made, ONE_HOT)
                for s in range(1, SETS, 2):
                    act.wait_ge(gram_full[1], t * SETS + (h * SETS // 2 + s // 2 + 1))
                    for j in range(PACK):
                        last = nc.scalar.activation(pairs_of(h, s, j), gram_of(1, j), ACT.Copy)
                    last.then_inc(gram_copied[1], 1)

            def relu1(n, at, size):
                for b in range(2):
                    act.wait_ge(l1_full, n * 2 + (b + 1))
                    for m in range(2):
                        last = nc.scalar.activation(h1[:, 2 * b + m, at:at + size], mlp_bank[b][:, m, at:at + size],
                                                    ACT.Relu, bias=b1[:, 2 * b + m:2 * b + m + 1])
                    last.then_inc(h1_made, 1)

            def relu2(n, at, size):
                act.wait_ge(l2_full, n + 1)
                for m in range(2):
                    last = nc.scalar.activation(h2[:, m, at:at + size], mlp_bank[0][:, m, at:at + size], ACT.Relu,
                                                bias=b2[:, m:m + 1])
                last.then_inc(h2_made, 1)

            def copy_y(n, size, later):
                act.wait_ge(l3_full, n + 1)
                if later:
                    act.wait_ge(y_stored, n * 16)
                nc.scalar.activation(y[0:1, 0:size], mlp_bank[1][0:1, 0, 0:size], ACT.Copy).then_inc(y_made, 1)

            make_high(0)
            act.wait_ge(hot_ids_loaded, 16)
            nc.scalar.activation(hot_f[:, :, :], hot_i[:, :, :], ACT.Copy).then_inc(hot_ids_cast, 1)
            for k in range(ONE_HOT):
                if k + 1 < ONE_HOT:
                    make_high(k + 1)

            copy_columns(0, 0, LOOKUPS)
            copy_columns(0, G0, HALF0)
            cast_ids(1)
            copy_pairs(0, 0, False)
            copy_columns(0, G1, HALF1)
            copy_pairs(0, 1, False)
            act.wait_ge(weights_loaded, 16 * WEIGHT_LOADS)

            def tile(t, y_later):
                copy_columns(t, 0, LOOKUPS)
                copy_columns(t, G0, HALF0)
                cast_ids(t + 1)
                relu1(t - 1, 0, TILE)
                copy_pairs(t, 0, True)
                copy_columns(t, G1, HALF1)
                relu2(t - 1, 0, TILE)
                copy_pairs(t, 1, True)
                copy_y(t - 1, TILE, y_later)

            tile(1, False)
            with act.Fori(2, TILES - 1) as t:
                tile(t, True)
            end = TILES - 1
            copy_columns(end, 0, LOOKUPS)
            copy_columns(end, G0, HALF0)
            relu1(end - 1, 0, TILE)
            copy_pairs(end, 0, True)
            relu2(end - 1, 0, TILE)
            copy_y(end - 1, TILE, True)
            relu1(end, 0, HALF)
            relu2(end, 0, HALF)
            copy_y(end, HALF, True)
            copy_columns(end, G1, HALF1)
            copy_pairs(end, 1, True)
            relu1(end + 1, HALF, HALF)
            relu2(end + 1, HALF, HALF)
            copy_y(end + 1, HALF, True)

        @block.vector
        def _(dve):
            nc.vector.memset(eT[:, :, F:PAD], 0.0).then_inc(pads_cleared, 1)

            def make_mask(t, k, chunks, later=True):
                if chunks[0] == 0:
                    dve.wait_ge(hot_ids_cast, t + 1)
                    if k >= MASKS:
                        dve.wait_ge(looked_up, t * ONE_HOT + (k - MASKS + 1))
                    elif later:
                        before = max(range(k, ONE_HOT, MASKS))
                        dve.wait_ge(looked_up, t * ONE_HOT - (ONE_HOT - before - 1))
                for c in chunks:
                    last = nc.vector.tensor_scalar(mask[0:ROWS, k % MASKS, c, :], hot_f[0:ROWS, k, :],
                                                   rowid[0:ROWS, c:c + 1], None, ALU.is_equal)
                if chunks[-1] == CHUNKS - 1:
                    last.then_inc(masks_made, 1)

            dve.wait_ge(rowid_loaded, 16)
            for k in range(ONE_HOT):
                table = stage[0:ROWS, k % STAGES, :]
                dve.wait_ge(high_made, k + 1)
                nc.vector.tensor_tensor(parts[0:ROWS, k, 1, :], table, parts[0:ROWS, k, 0, :].bitcast(fp32), ALU.subtract)\
                    .then_inc(low_made, 1)
                if k < MASKS:
                    make_mask(0, k, range(CHUNKS), False)

            def copy_columns(t, first, groups, masks_from=ONE_HOT):
                k = masks_from
                for g, group in enumerate(groups, first):
                    if g % 2 == 0:
                        while k < min(ONE_HOT, group[2] + MASKS):
                            make_mask(t, k, range(CHUNKS))
                            k += 1
                        dve.wait_ge(*fill_signal(t, g, group))
                        nc.vector.tensor_copy(columns_of(group), filled(0, group)).then_inc(col_copied[0], 1)

            def copy_pairs(t, h, later, with_masks):
                if later:
                    dve.wait_ge(x_loaded[h], t * (16 * len(BLOCKS)))
                for s in range(0, SETS, 2):
                    dve.wait_ge(gram_full[0], t * SETS + (h * SETS // 2 + s // 2 + 1))
                    for j in range(PACK):
                        last = nc.vector.tensor_copy(pairs_of(h, s, j), gram_of(0, j))
                    last.then_inc(gram_copied[0], 1)
                    if with_masks:
                        make_mask(t + 1, h, range(s * 2, s * 2 + 4))

            def tile(t, later, last):
                copy_columns(t, 0, LOOKUPS, 2 if later else MASKS)
                copy_columns(t, G0, HALF0)
                copy_pairs(t, 0, later, not last)
                copy_columns(t, G1, HALF1)
                copy_pairs(t, 1, later, not last)

            tile(0, False, False)
            dve.wait_ge(weights_loaded, 16 * WEIGHT_LOADS)
            nc.vector.tensor_tensor(w1[:, X_CHUNKS, :], w1[:, X_CHUNKS, :], wb[:, :], ALU.add).then_inc(w1_summed, 1)
            with dve.Fori(1, TILES - 1) as t:
                tile(t, True, False)
            tile(TILES - 1, True, True)

        @block.tensor
        def _(pe):
            def look_up(t, later):
                for g, (_, _, f, n) in enumerate(LOOKUPS):
                    b = g % 2
                    if later or g >= 2:
                        pe.wait_ge(col_copied[b], t * PER_BANK + g // 2)
                    for i in range(n):
                        k = f + i
                        if not later:
                            pe.wait_ge(low_made, k + 1)
                        pe.wait_ge(masks_made, t * ONE_HOT + (k + 1))
                        for c in range(CHUNKS):
                            for part in range(PARTS):
                                last = nc.tensor.matmul(
                                    col_bank[b][:, i * TILE:(i + 1) * TILE], parts[0:ROWS, k, part, c * D:(c + 1) * D],
                                    mask[0:ROWS, k % MASKS, c, :], start=(c == 0 and part == 0),
                                    stop=(c == CHUNKS - 1 and part == PARTS - 1))
                        last.then_inc(looked_up, 1)

            def transpose_rows(t, g, group, first):
                _, h, f, n = group
                if first:
                    pe.wait_ge(gathered[h], t * (16 * GATHERED) + 16 * GATHERED)
                pe.wait_ge(col_copied[g % 2], t * PER_BANK + g // 2)
                for i in range(n):
                    last = nc.tensor.transpose(col_bank[g % 2][:, i * HALF:(i + 1) * HALF],
                                               rows[:, h, (f + i) * D:(f + i + 1) * D], ident[:, :])
                last.then_inc(half_transposed[h] if f + n == GATHERED else col_full[g % 2], 1)

            def transposes(t, g, groups, between):
                for i, group in enumerate(groups):
                    transpose_rows(t, g + i, group, i == 0)
                    if i % 2 == 1 and between:
                        between.pop(0)()
                for step in between:
                    step()

            def multiply_pairs(t, h, later):
                fills = G1 if h == 0 else FILLS
                pe.wait_ge(col_copied[0], t * PER_BANK + (fills + 1) // 2)
                pe.wait_ge(col_copied[1], t * PER_BANK + fills // 2)
                for s in range(SETS):
                    n = h * SETS // 2 + s // 2
                    if later or n > 0:
                        pe.wait_ge(gram_copied[s % 2], t * SETS + n)
                    for q in range(SET // PACK):
                        a = h * HALF + s * SET + q * PACK
                        last = nc.tensor.matmul(
                            gram_bank[s % 2][0:GRAM_ROWS, q, 0:PACK * (F - 1)],
                            eT[:, a:a + PACK, :].rearrange("p s f -> p (s f)")[:, 0:GRAM_ROWS],
                            eT[:, a:a + PACK, 1:F], start=True, stop=True)
                    last.then_inc(gram_full[s % 2], 1)

            def layer1(n, blocks, at, size, later):
                for m in blocks:
                    if m == 2 and later:
                        pe.wait_ge(y_made, n)
                    for c in [X_CHUNKS, *range(X_CHUNKS)]:
                        k = X_ROWS[c] if c < X_CHUNKS else D
                        last = nc.tensor.matmul(mlp_bank[m // 2][:, m % 2, at:at + size], w1[0:k, c, m * 128:(m + 1) * 128],
                                                x[0:k, c, at:at + size], start=(c == X_CHUNKS), stop=(c == X_CHUNKS - 1))
                    if m % 2 == 1:
                        last.then_inc(l1_full, 1)

            def layer2(n, blocks, at, size):
                for m in blocks:
                    if m == 0:
                        pe.wait_ge(h1_made, n * 2 + 2)
                    for c in range(N1 // 128):
                        last = nc.tensor.matmul(mlp_bank[0][:, m, at:at + size], w2[:, c, m * 128:(m + 1) * 128],
                                                h1[:, c, at:at + size], start=(c == 0), stop=(c == N1 // 128 - 1))
                    if m == 1:
                        last.then_inc(l2_full, 1)

            def layer3(n, at, size):
                pe.wait_ge(h2_made, n + 1)
                for c in range(N2 // 128):
                    last = nc.tensor.matmul(mlp_bank[1][0:1, 0, 0:size], w3[:, c:c + 1], h2[:, c, at:at + size],
                                            start=(c == 0), stop=(c == N2 // 128 - 1))
                last.then_inc(l3_full, 1)

            def x_ready(t, halves):
                for h in halves:
                    pe.wait_ge(x_loaded[h], t * (16 * len(BLOCKS)) + 16 * len(BLOCKS))
                pe.wait_ge(bottom_loaded, t * 16 + 16)

            look_up(0, False)
            pe.wait_ge(ident_loaded, 16)
            transposes(0, G0, HALF0, [])
            pe.wait_ge(pads_cleared, 1)
            multiply_pairs(0, 0, False)
            transposes(0, G1, HALF1, [])
            multiply_pairs(0, 1, False)
            pe.wait_ge(weights_loaded, 16 * WEIGHT_LOADS)
            pe.wait_ge(w1_summed, 1)

            def tile(t, l1_later):
                look_up(t, True)
                x_ready(t - 1, range(2))
                transposes(t, G0, HALF0, [lambda m=m: layer1(t - 1, [m], 0, TILE, l1_later) for m in range(4)])
                multiply_pairs(t, 0, True)
                transposes(t, G1, HALF1, [lambda m=m: layer2(t - 1, [m], 0, TILE) for m in range(2)])
                multiply_pairs(t, 1, True)
                layer3(t - 1, 0, TILE)

            tile(1, False)
            with pe.Fori(2, TILES - 1) as t:
                tile(t, True)
            end = TILES - 1
            look_up(end, True)
            x_ready(end - 1, range(2))
            transposes(end, G0, HALF0, [lambda m=m: layer1(end - 1, [m], 0, TILE, True) for m in range(4)])
            multiply_pairs(end, 0, True)
            layer2(end - 1, range(2), 0, TILE)
            layer3(end - 1, 0, TILE)
            x_ready(end, [0])
            layer1(end, range(4), 0, HALF, True)
            layer2(end, range(2), 0, HALF)
            layer3(end, 0, HALF)
            transposes(end, G1, HALF1, [])
            multiply_pairs(end, 1, True)
            x_ready(end, [1])
            layer1(end + 1, range(4), HALF, HALF, True)
            layer2(end + 1, range(2), HALF, HALF)
            layer3(end + 1, HALF, HALF)


def kernel(**inputs):
    import numpy as np
    import concourse.bacc as bacc
    from concourse.bass_utils import run_bass_kernel_spmd

    nc = bacc.Bacc("TRN2", target_bir_lowering=False, num_devices=1)
    arrays = {}

    def put(name, a):
        a = np.ascontiguousarray(a)
        arrays[name] = a
        return nc.dram_tensor(name, a.shape, mybir.dt.from_np(a.dtype), kind="ExternalInput").ap()

    ids = np.asarray(inputs["ids"])
    w_top1 = np.asarray(inputs["W_top1"])
    w1_pairs = np.zeros((max(X_ROWS), X_CHUNKS, N1), w_top1.dtype)
    for (first, n), row in zip(BLOCKS, BLOCK_ROW):
        for i in range(max(first, 1), first + X_CHUNKS):
            for j in range(i):
                a, b = max(ORDER[i], ORDER[j]), min(ORDER[i], ORDER[j])
                w1_pairs[row + j, i - first] = w_top1[D + a * (a - 1) // 2 + b]
    tables = [put(f"in_tbl_{f}", inputs[f"tbl_{f}"]) for f in range(F)]
    args = [
        put("in_gather_ids", ids[:, GATHERED_TABLES].reshape(B // HALF, HALF, GATHERED)),
        put("in_hot_ids", ids[:, ONE_HOT_TABLES].reshape(TILES, TILE, ONE_HOT).transpose(0, 2, 1)),
        put("in_bottom", np.asarray(inputs["r_bottom_mlp_out"]).T),
        put("in_w1_pairs", w1_pairs.reshape(-1, X_CHUNKS * N1)),
        put("in_w1_bottom_a", w_top1[0:D]),
        put("in_w1_bottom_b", w_top1[D + PAIRS:]),
        put("in_b1", np.asarray(inputs["b_top1"]).reshape(N1 // 128, 128).T),
        put("in_w2", inputs["W_top2"]),
        put("in_b2", np.asarray(inputs["b_top2"]).reshape(N2 // 128, 128).T),
        put("in_w3", np.asarray(inputs["W_top3"]).reshape(N2 // 128, 128).T),
        put("in_identity", np.eye(128, dtype=np.float32)),
        put("in_row_of_chunk", np.arange(128 * CHUNKS, dtype=np.float32).reshape(128, CHUNKS)),
    ]
    out = nc.dram_tensor("out_y", (1, B), mybir.dt.float32, kind="ExternalOutput").ap()
    build(nc, tables, *args, out)
    r = run_bass_kernel_spmd(nc, [arrays], core_ids=[0])
    return r.results[0]["out_y"].reshape(B, 1)
```
